# Optimizing a Trainium2 kernel written in Bass

```python
import numpy as np
import jax
import jax.numpy as jnp

def _softmax(x, axis=-1):
    return jax.nn.softmax(x, axis=axis)

def _gelu(x):
    return jax.nn.gelu(x, approximate=True)

def _silu(x):
    return jax.nn.silu(x)

def _sigmoid(x):
    return jax.nn.sigmoid(x)

def _layernorm(x, axis=-1, eps=1e-05):
    m = jnp.mean(x, axis=axis, keepdims=True)
    v = jnp.var(x, axis=axis, keepdims=True)
    return (x - m) / jnp.sqrt(v + eps)

def _scatter_add(tgt, idx, src, axis=0):
    return tgt.at[idx].add(src)

def _segment_sum(src, seg, n):
    return jax.ops.segment_sum(src, seg, n)
kernel_name = 'mk_decoder_preln_d1_seqx_r8_d0443a'

def setup_inputs(seed: int=0):
    np.random.seed(seed)
    _w = jnp.asarray

    def _rec_inputs():
        import jax
        import jax.numpy as jnp
        _rk = jax.random.key(seed)
        x = 7.22e-05 + 1 * jax.random.normal(jax.random.fold_in(_rk, 1), (64, 64, 256), jnp.float32)
        _lenS = 64 - jax.random.randint(jax.random.fold_in(_rk, 7), (64,), 0, max(1, 64 // 4) + 1, jnp.int32)
        _lenS2 = 64 - jax.random.randint(jax.random.fold_in(_rk, 8), (64,), 0, max(1, 64 // 4) + 1, jnp.int32)
        _ctx_2048P = jax.random.normal(jax.random.fold_in(_rk, 11), (64, 16, 256), jnp.float32)
        _ctx_2048c = jax.random.dirichlet(jax.random.fold_in(_rk, 511), 0.3 * jnp.ones((16,), jnp.float32), (64, 64))
        _ctx_2048t = jnp.einsum('bsk,bkd->bsd', _ctx_2048c, _ctx_2048P)
        _ctx_2048t = _ctx_2048t * jax.lax.rsqrt(jnp.mean(jnp.square(_ctx_2048t)) + 1e-12) * 0.953939
        ctx_2048 = 4.13588e-05 + 0.999923 * (_ctx_2048t + 0.3 * jax.random.normal(jax.random.fold_in(_rk, 611), (64, 64, 256), jnp.float32))
        return (x, ctx_2048)
    x, ctx_2048 = _rec_inputs()

    def _L0_attn_setup():
        import jax, jax.numpy as jnp
        import numpy as np
        import math
        B, T = (4, 128)
        D_MODEL = 256
        HEAD_DIM = 64
        N_HEADS = 32
        N_KV = 8
        Q_MULT = N_HEADS // N_KV
        SLIDING_WINDOW = 128
        CAUSAL = True
        SM_SCALE = 1.0 / math.sqrt(HEAD_DIM)
        ROPE_THETA = 150000.0
        SCALING = 32.0
        NTK_ALPHA = 1.0
        NTK_BETA = 32.0
        ICL = 128

        def _rope_cos_sin(t_len):
            d_half = HEAD_DIM // 2
            freq = ROPE_THETA ** (np.arange(0, HEAD_DIM, 2, dtype=np.float32) / HEAD_DIM)
            concentration = 0.1 * math.log(SCALING) + 1.0
            low = d_half * math.log(ICL / (NTK_BETA * 2 * math.pi)) / math.log(ROPE_THETA)
            high = d_half * math.log(ICL / (NTK_ALPHA * 2 * math.pi)) / math.log(ROPE_THETA)
            interpolation = 1.0 / (SCALING * freq)
            extrapolation = 1.0 / freq
            ramp = np.clip((np.arange(d_half, dtype=np.float32) - low) / (high - low), 0.0, 1.0)
            mask = 1.0 - ramp
            inv_freq = interpolation * (1.0 - mask) + extrapolation * mask
            freqs = np.outer(np.arange(t_len, dtype=np.float32), inv_freq)
            return (jnp.asarray(np.cos(freqs) * concentration, jnp.float32), jnp.asarray(np.sin(freqs) * concentration, jnp.float32))

        def _apply_rope(x, cos, sin):
            x1, x2 = jnp.split(x, 2, axis=-1)
            return jnp.concatenate([x1 * cos - x2 * sin, x2 * cos + x1 * sin], axis=-1)
        key = jax.random.key(seed)
        ks = jax.random.split(key, 6)
        qkv_dim = HEAD_DIM * (N_HEADS + 2 * N_KV)
        return {'x': jax.random.normal(ks[0], (B, T, D_MODEL), jnp.float32), 'qkv_w': jax.random.normal(ks[1], (qkv_dim, D_MODEL), jnp.float32) * 0.02, 'qkv_b': jax.random.normal(ks[2], (qkv_dim,), jnp.float32) * 0.02, 'out_w': jax.random.normal(ks[3], (D_MODEL, N_HEADS * HEAD_DIM), jnp.float32) * 0.02, 'out_b': jax.random.normal(ks[4], (D_MODEL,), jnp.float32) * 0.02, 'sinks': jax.random.normal(ks[5], (N_HEADS,), jnp.float32) * (1.0 / math.sqrt(HEAD_DIM))}
    _L0_attn_all = _L0_attn_setup()
    _L0_attn_in = {k: v for k, v in _L0_attn_all.items() if k in ('qkv_w', 'qkv_b', 'out_w', 'out_b', 'sinks')}
    del _L0_attn_all

    def _L0_xattn_setup():
        import jax, jax.numpy as jnp
        import numpy as np
        N_HEAD = 8
        key = jax.random.key(seed)
        k1, k2, k3 = jax.random.split(key, 3)
        b, d, m = (4, 128, 256)
        c, n = (128, 256)
        q = jax.random.normal(k1, (b, d, m), dtype=jnp.float32)
        k = jax.random.normal(k2, (d // d * b, d, n), dtype=jnp.float32).reshape(b, d, n)
        v = jax.random.normal(k3, (b, c, n), dtype=jnp.float32)
        return {'q': q, 'k': k, 'v': v}
    _L0_xattn_all = _L0_xattn_setup()
    _L0_xattn_in = {k: v for k, v in _L0_xattn_all.items() if k in ()}
    del _L0_xattn_all

    def _L0_ffn_setup():
        import jax, jax.numpy as jnp
        import numpy as np
        E, H, I = (8, 256, 512)
        TOP_K = 1
        B, S = (1, 256)
        key = jax.random.key(seed)
        ks = jax.random.split(key, 7)
        std = 0.02
        return {'hidden_states': jax.random.normal(ks[0], (B, S, H), dtype=jnp.float32), 'router_w': jax.random.normal(ks[1], (E, H), dtype=jnp.float32) * std, 'gate_up_proj': jax.random.normal(ks[2], (E, H, 2 * I), dtype=jnp.float32) * std, 'down_proj': jax.random.normal(ks[3], (E, I, H), dtype=jnp.float32) * std, 'shared_gate_w': jax.random.normal(ks[4], (H, I), dtype=jnp.float32) * std, 'shared_up_w': jax.random.normal(ks[5], (H, I), dtype=jnp.float32) * std, 'shared_down_w': jax.random.normal(ks[6], (I, H), dtype=jnp.float32) * std}
    _L0_ffn_all = _L0_ffn_setup()
    _L0_ffn_in = {k: v for k, v in _L0_ffn_all.items() if k in ('router_w', 'gate_up_proj', 'down_proj', 'shared_gate_w', 'shared_up_w', 'shared_down_w')}
    del _L0_ffn_all
    return {'x': x, 'ctx_2048': ctx_2048, 'L0_attn_qkv_w': _L0_attn_in['qkv_w'], 'L0_attn_qkv_b': _L0_attn_in['qkv_b'], 'L0_attn_out_w': _L0_attn_in['out_w'], 'L0_attn_out_b': _L0_attn_in['out_b'], 'L0_attn_sinks': _L0_attn_in['sinks'], 'L0_ffn_router_w': _L0_ffn_in['router_w'], 'L0_ffn_gate_up_proj': _L0_ffn_in['gate_up_proj'], 'L0_ffn_down_proj': _L0_ffn_in['down_proj'], 'L0_ffn_shared_gate_w': _L0_ffn_in['shared_gate_w'], 'L0_ffn_shared_up_w': _L0_ffn_in['shared_up_w'], 'L0_ffn_shared_down_w': _L0_ffn_in['shared_down_w']}

def reference(x, ctx_2048, L0_attn_qkv_w, L0_attn_qkv_b, L0_attn_out_w, L0_attn_out_b, L0_attn_sinks, L0_ffn_router_w, L0_ffn_gate_up_proj, L0_ffn_down_proj, L0_ffn_shared_gate_w, L0_ffn_shared_up_w, L0_ffn_shared_down_w):
    import jax
    import jax.numpy as jnp

    def _L0_attn_ref(x, qkv_w, qkv_b, out_w, out_b, sinks):
        import jax, jax.numpy as jnp
        import numpy as np
        import math
        B, T = (4, 128)
        D_MODEL = 256
        HEAD_DIM = 64
        N_HEADS = 32
        N_KV = 8
        Q_MULT = N_HEADS // N_KV
        SLIDING_WINDOW = 128
        CAUSAL = True
        SM_SCALE = 1.0 / math.sqrt(HEAD_DIM)
        ROPE_THETA = 150000.0
        SCALING = 32.0
        NTK_ALPHA = 1.0
        NTK_BETA = 32.0
        ICL = 128

        def _rope_cos_sin(t_len):
            d_half = HEAD_DIM // 2
            freq = ROPE_THETA ** (np.arange(0, HEAD_DIM, 2, dtype=np.float32) / HEAD_DIM)
            concentration = 0.1 * math.log(SCALING) + 1.0
            low = d_half * math.log(ICL / (NTK_BETA * 2 * math.pi)) / math.log(ROPE_THETA)
            high = d_half * math.log(ICL / (NTK_ALPHA * 2 * math.pi)) / math.log(ROPE_THETA)
            interpolation = 1.0 / (SCALING * freq)
            extrapolation = 1.0 / freq
            ramp = np.clip((np.arange(d_half, dtype=np.float32) - low) / (high - low), 0.0, 1.0)
            mask = 1.0 - ramp
            inv_freq = interpolation * (1.0 - mask) + extrapolation * mask
            freqs = np.outer(np.arange(t_len, dtype=np.float32), inv_freq)
            return (jnp.asarray(np.cos(freqs) * concentration, jnp.float32), jnp.asarray(np.sin(freqs) * concentration, jnp.float32))

        def _apply_rope(x, cos, sin):
            x1, x2 = jnp.split(x, 2, axis=-1)
            return jnp.concatenate([x1 * cos - x2 * sin, x2 * cos + x1 * sin], axis=-1)
        Bv, Tv, _ = x.shape
        qkv = x @ qkv_w.T + qkv_b
        q = qkv[..., :N_HEADS * HEAD_DIM].reshape(Bv, Tv, N_KV, Q_MULT, HEAD_DIM)
        k = qkv[..., N_HEADS * HEAD_DIM:(N_HEADS + N_KV) * HEAD_DIM].reshape(Bv, Tv, N_KV, HEAD_DIM)
        v = qkv[..., (N_HEADS + N_KV) * HEAD_DIM:].reshape(Bv, Tv, N_KV, HEAD_DIM)
        cos, sin = _rope_cos_sin(Tv)
        q = _apply_rope(q, cos[:, None, None, :], sin[:, None, None, :])
        k = _apply_rope(k, cos[:, None, :], sin[:, None, :])
        logits = jnp.einsum('bqhmd,bkhd->bhmqk', q, k) * SM_SCALE
        i = jnp.arange(Tv)[:, None]
        j = jnp.arange(Tv)[None, :]
        mask = jnp.zeros((Tv, Tv), dtype=bool)
        if CAUSAL:
            mask = mask | (j > i)
        if SLIDING_WINDOW > 0:
            mask = mask | (j <= i - SLIDING_WINDOW)
        logits = jnp.where(mask, -jnp.inf, logits)
        m = jnp.max(logits, axis=-1, keepdims=True)
        e = jnp.exp(logits - m)
        s = sinks.reshape(N_KV, Q_MULT)[None, :, :, None, None]
        exp_sink = jnp.exp(s - m)
        w = e / (jnp.sum(e, axis=-1, keepdims=True) + exp_sink)
        out = jnp.einsum('bhmqk,bkhd->bqhmd', w, v).reshape(Bv, Tv, N_HEADS * HEAD_DIM)
        return out @ out_w.T + out_b

    def _L0_xattn_ref(q, k, v):
        import jax, jax.numpy as jnp
        import numpy as np
        N_HEAD = 8
        b, d, m = q.shape
        c = v.shape[1]
        h = N_HEAD
        qh = q.reshape(b * h, d // h, m)
        kh = k.reshape(b * h, d // h, -1)
        vh = v.reshape(b * h, c // h, -1)
        scale = 1.0 / jnp.sqrt(jnp.asarray(d // h, dtype=q.dtype))
        qk = jnp.einsum('bdm,bdn->bmn', qh, kh) * scale
        sm = jax.nn.softmax(qk, axis=-1)
        ret = jnp.einsum('bmn,bcn->bcm', sm, vh)
        return ret.reshape(b, c, m)

    def _L0_ffn_ref(hidden_states, router_w, gate_up_proj, down_proj, shared_gate_w, shared_up_w, shared_down_w):
        import jax, jax.numpy as jnp
        import numpy as np
        E, H, I = (8, 256, 512)
        TOP_K = 1
        B, S = (1, 256)
        orig_shape = hidden_states.shape
        x = hidden_states.reshape(-1, H)
        T = x.shape[0]
        logits = x @ router_w.T
        top_vals, top_idx = jax.lax.top_k(logits, TOP_K)
        scores = jnp.full_like(logits, -jnp.inf)
        scores = scores.at[jnp.arange(T)[:, None], top_idx].set(top_vals)
        scores = jax.nn.sigmoid(scores.astype(jnp.float32)).astype(logits.dtype)
        xr = x[None, :, :] * scores.T[:, :, None]
        gate_up = jnp.einsum('eth,ehf->etf', xr, gate_up_proj)
        gate, up = jnp.split(gate_up, 2, axis=-1)
        routed = jnp.einsum('etf,efh->eth', up * jax.nn.silu(gate), down_proj)
        routed_sum = routed.sum(axis=0)
        shared = jax.nn.silu(x @ shared_gate_w) * (x @ shared_up_w) @ shared_down_w
        return (shared + routed_sum).reshape(orig_shape)
    x = x + _L0_attn_ref(_layernorm(x, axis=-1), L0_attn_qkv_w, L0_attn_qkv_b, L0_attn_out_w, L0_attn_out_b, L0_attn_sinks)
    x = x + _L0_xattn_ref(_layernorm(x, axis=-1), ctx_2048, ctx_2048)
    x = x + _L0_ffn_ref(_layernorm(x, axis=-1), L0_ffn_router_w, L0_ffn_gate_up_proj, L0_ffn_down_proj, L0_ffn_shared_gate_w, L0_ffn_shared_up_w, L0_ffn_shared_down_w)
    return x

_drawn_inputs = setup_inputs


def setup_inputs(seed=0):
    import zlib

    import numpy as np

    out = dict(_drawn_inputs(seed))
    spreads = {}
    factors = {'L0_attn_sinks': 8.0,
     'L0_ffn_router_w': 8.0,
     'L0_ffn_gate_up_proj': 8.0,
     'L0_ffn_down_proj': 8.0,
     'L0_ffn_shared_gate_w': 3.319,
     'L0_ffn_shared_up_w': 3.294,
     'L0_ffn_shared_down_w': 3.273}
    for name, (base, spread) in spreads.items():
        noise = np.random.default_rng([zlib.crc32(name.encode()), seed]).standard_normal(out[name].shape)
        drawn = base * np.exp(spread * noise) if base else spread * noise
        out[name] = jnp.asarray(drawn.astype(out[name].dtype))
    for name, factor in factors.items():
        out[name] = (out[name] * factor).astype(out[name].dtype)
    return out
```

```python
import math
from contextlib import ExitStack

import numpy as np

import concourse.bass as bass
from concourse import mybir

F32 = mybir.dt.float32
F32R = mybir.dt.float32r
BF16 = mybir.dt.bfloat16
I32 = mybir.dt.int32
U32 = mybir.dt.uint32
ALU = mybir.AluOpType
ACT = mybir.ActivationFunctionType
AX = mybir.AxisListType

P = 128
T = 64
D = 256
HD = 64
NH, NKV = 32, 8
NPAIR = NH // 2
XH = 16
MR = 32 + XH
XD = 8
E = 8
FF = 512
WE = 2 * 2 * FF + 4 * D
EPS = 1e-5
BIG = 1 << 20

CONST = {}
_at = 0
for _name, _n in (("ident", P), ("tri", P), ("mask", 512), ("cosq", HD), ("sinq", HD), ("cosk", HD), ("sink", HD),
                  ("rowsel", 3), ("iota8", E), ("base", E), ("thr", 64), ("pidx", 1), ("shw", 1),
                  ("sel", XH)):
    CONST[_name] = (_at, _at + _n)
    _at += _n
NCONST = _at


def constants(cap, nrt):
    c = np.zeros((P, NCONST), np.float32)

    def put(name, v):
        a, b = CONST[name]
        c[:, a:b] = v

    p = np.arange(P)
    put("ident", np.eye(P))
    put("sel", (p % 32)[:, None] == np.arange(XH))
    put("tri", (p[:, None] <= p[None, :]))
    put("mask", np.where((np.arange(512) % T)[None, :] > (p % T)[:, None], -1e30, 0.0))
    half = HD // 2
    freq = 150000.0 ** (np.arange(0, HD, 2, dtype=np.float32) / HD)
    conc = 0.1 * math.log(32.0) + 1.0
    low = half * math.log(128 / (32.0 * 2 * math.pi)) / math.log(150000.0)
    high = half * math.log(128 / (1.0 * 2 * math.pi)) / math.log(150000.0)
    ramp = np.clip((np.arange(half, dtype=np.float32) - low) / (high - low), 0.0, 1.0)
    keep = 1.0 - ramp
    inv = 1.0 / (32.0 * freq) * (1.0 - keep) + 1.0 / freq * keep
    ang = np.outer(np.arange(T, dtype=np.float32), inv)
    cos = (np.cos(ang) * conc).astype(np.float32)[p % T]
    sin = (np.sin(ang) * conc).astype(np.float32)[p % T]
    scale = np.float32(1.0 / math.sqrt(HD))
    put("cosq", np.concatenate([cos, cos], 1) * scale)
    put("sinq", np.concatenate([-sin, sin], 1) * scale)
    put("cosk", np.concatenate([cos, cos], 1))
    put("sink", np.concatenate([-sin, sin], 1))
    put("rowsel", np.eye(P)[:, :3])
    put("iota8", np.arange(E)[None])
    put("base", (np.arange(E) * cap - 1)[None])
    put("thr", (128 * np.arange(64))[None])
    put("pidx", p[:, None])
    put("shw", np.where(p >= nrt, WE, 0)[:, None])
    return c


def back(tile, n):
    h, p = tile
    for _ in range(n):
        h, p = (h, 0) if p else (h - 1, 1)
    return h, p


def ahead(tile):
    h, p = tile
    return (h + 1, 0) if p else (h, 1)


def num(tile):
    return tile[0] * 2 + tile[1]


def need(eng, sem, value):
    if isinstance(value, int) and value <= 0:
        return
    eng.wait_ge(sem, value)


def in_loop(tile):
    return not isinstance(num(tile), int)


class Chain:

    def __init__(self, eng, sem, per, tile):
        self.eng, self.sem, self.per, self.n, self.t = eng, sem, per, 0, num(tile)

    def __call__(self, ins):
        self.n += 1
        ins.then_inc(self.sem, 1)
        self.eng.wait_ge(self.sem, self.t * self.per + self.n)

    def end(self):
        assert self.n == self.per, (self.n, self.per)


def decoder(nc, A, NT, NRT):
    CAP = NT * P
    DUMMY = E * CAP
    XROWS = DUMMY + (NRT - NT) * P
    FIRST, LAST = 4, NT - 2
    NALL = NRT + NT
    assert NT % 2 == 0 and NT >= 4 and NRT % 2 == 0 and NALL < P

    def dram(name, shape, dt=F32):
        return nc.dram_tensor(name, shape, dt, kind="Internal").ap()

    stackq_d = [dram(f"stackq_d{p}", (XH, 3, XD, D)) for p in range(2)]
    stackk_d = [dram(f"stackk_d{p}", (XH, 3, XD, D)) for p in range(2)]
    xg_d = dram("xg_d", (XROWS, D))
    yg_d = dram("yg_d", (NRT * P, D))
    xn3_d = dram("xn3_d", (NT * P, D))
    x2_d = dram("x2_d", (NT * P, D))
    tab_d = dram("tab_d", (P, 2), I32)

    top = ExitStack()
    with top:
        def sem(name):
            return top.enter_context(nc.semaphore(name))

        def sb_top(name, shape, dt=F32):
            return top.enter_context(nc.sbuf_tensor(name, shape, dt))

        def bank(name, n=1):
            return top.enter_context(nc.psum_tensor(name, [P, n, 512], F32))

        const = sb_top("const", [P, NCONST])
        posall = sb_top("posall", [P, NT])
        run = sb_top("run", [P, E])
        zeros = sb_top("zeros", [P, D])
        C = {k: const[:, a:b] for k, (a, b) in CONST.items()}
        ident = C["ident"]

        bk = [bank(f"bank{i}") for i in range(2)]
        bS = bank("bankS", 2)
        b4 = bank("bank4")
        bX = bank("bankX", 2)
        b7 = bank("bank7")

        with ExitStack() as pa:
            def sb(name, shape, dt=F32):
                return pa.enter_context(nc.sbuf_tensor(name, shape, dt))

            wqh, wql = (sb(n, [P, 2, 3072], F32R) for n in ("wqh", "wql"))
            woh, wol = (sb(n, [P, NPAIR, D], F32R) for n in ("woh", "wol"))
            bias3 = sb("bias3", [P, 3072 + D], BF16)
            identb = sb("identb", [P, P], BF16)
            onesb = sb("onesb", [P, P], BF16)
            onesf = sb("onesf", [P, P])
            maskb = sb("maskb", [P, 512], BF16)
            sinks = sb("sinks", [P, 2, 16])
            half_neg = sb("half_neg", [P, 1])
            spare_g, spare_v = sb("spare_g", [P, 1]), sb("spare_v", [P, 1])
            rw = sb("rw", [P, 2, E])

            x = [sb(f"x{p}", [P, D]) for p in range(2)]
            ctx = [sb(f"ctx{p}", [P, D]) for p in range(2)]
            xn = sb("xn", [P, D])
            xnTh, xnTl = (sb(n, [P, 2, P], F32R) for n in ("xnTh", "xnTl"))
            stats = sb("stats", [P, 3, 6])
            mv = sb("mv", [P, 3, 2])
            rstd = sb("rstd", [P, 3, 2])
            vbd = [sb(f"vbd{b}", [P, NKV // 2, P]) for b in range(2)]
            cT = sb("cT", [P, 2, XH, P + XD])
            selh = sb("selh", [MR, XH, P], F32R)
            xmaxT = sb("xmaxT", [MR, D], F32R)
            with nc.sbuf_tensor("stage", [P, 2, 2048], F32) as stage, \
                    nc.sbuf_tensor("brow", [P, 3072 + D], F32) as brow, \
                    nc.sbuf_tensor("btmp", [P, 3072 + D], BF16) as btmp:
                pass
            ropeC = [sb(f"ropeC{p}", [P, 512]) for p in range(2)]
            ropeD = [sb(f"ropeD{p}", [P, 512]) for p in range(2)]
            qT = sb("qT", [P, NPAIR, P])
            kT = sb("kT", [P, NKV // 2, P])
            prob = sb("prob", [P, 2, 16 * HD + 16])
            mx = sb("mx", [P, 2, 16])
            den = sb("den", [P, 2, 16])
            dsum = sb("dsum", [P, 2, 16])
            rden = sb("rden", [P, 2, 16])
            probT = [sb(f"probT{g}", [P, 4, P]) for g in range(2)]
            oTh = [sb(f"oTh{g}", [P, 4, P], F32R) for g in range(2)]
            oTl = [sb(f"oTl{g}", [P, 4, P], F32R) for g in range(2)]
            x1 = [sb(f"x1_{p}", [P, D]) for p in range(2)]
            q2 = sb("q2", [P, D])
            q2hl = sb("q2hl", [P, 2, D], F32R)
            chl = sb("chl", [P, 2, D], F32R)
            stq = [sb(f"stq{p}", [P, 4, D], F32R) for p in range(2)]
            stk = [sb(f"stk{p}", [P, 4, D], F32R) for p in range(2)]
            xmax = sb("xmax", [P, 2, XH])
            xsum = sb("xsum", [P, 2, XH])
            xlog = sb("xlog", [P, 2, XH])
            xshift = sb("xshift", [P, 2, XH])
            xe = [sb(f"xe{i}", [P, 2, D]) for i in range(2)]
            x2 = [sb(f"x2_{p}", [P, D]) for p in range(2)]
            xn3 = [sb(f"xn3_{p}", [P, D]) for p in range(2)]
            xr = [sb(f"xr{p}", [P, D]) for p in range(2)]
            xn3T = sb("xn3T", [P, 2, P])
            top8 = sb("top8", [P, 8])
            idx8 = sb("idx8", [P, 8], U32)
            posx = [sb(f"posx{p}", [P, 1], I32) for p in range(2)]
            idxf = sb("idxf", [P, 1])
            onehot = sb("onehot", [P, E])
            pos8 = sb("pos8", [P, E])
            posf = sb("posf", [P, 1])
            ptmp = sb("ptmp", [P, E])
            score = sb("score", [P, 4])

            s_const, s_zero = sem("s_const"), sem("s_zero")
            s_stage = [sem(f"s_stage{i}") for i in range(2)]
            s_hi, s_lo = sem("s_hi"), sem("s_lo")
            s_bias, s_setv, s_setg = sem("s_bias"), sem("s_setv"), sem("s_setg")
            s_x = [sem(f"s_xin_a{p}") for p in range(2)]
            s_ctx = [sem(f"s_ctx_a{p}") for p in range(2)]
            s_stw = [sem(f"s_stw{p}") for p in range(2)]
            s_str = [sem(f"s_str{p}") for p in range(2)]
            s_fst = [sem(f"s_fst{p}") for p in range(2)]
            s_scat = [sem(f"s_scat{p}") for p in range(2)]
            s_var = [sem(f"s_var{n}") for n in range(3)]
            s_rstd = [sem(f"s_rstd{n}") for n in range(3)]
            s_norm = [sem(f"s_norm{n}") for n in range(3)]
            c_ln = [sem(f"c_ln{n}") for n in range(3)]
            g_ln = [sem(f"g_ln{n}") for n in range(3)]
            s_xnTp, s_xnTh, s_xnT = sem("s_xnTp"), sem("s_xnTh"), sem("s_xnT")
            s_qkv, s_rope, s_v = sem("s_qkv"), sem("s_rope"), sem("s_v")
            s_turn, s_qkT = sem("s_turn"), sem("s_qkT")
            s_S, s_sub, s_exp, s_rden, s_pn = (sem(n) for n in ("s_S", "s_sub", "s_exp", "s_rden", "s_pn"))
            s_PTp, s_PT, s_pv, s_oh, s_o, s_out, s_x1 = (
                sem(n) for n in ("s_PTp", "s_PT", "s_pv", "s_oh", "s_o", "s_out", "s_x1"))
            c_soft = sem("c_soft")
            s_q2hl, s_chl = sem("s_q2hl"), sem("s_chl")
            g_c, g_q2 = sem("g_c"), sem("g_q2")
            s_cTp, s_cT = sem("s_cTp"), sem("s_cT")
            s_xs, s_xm, s_xsum, s_xlog, s_shift, s_mt, s_mh, s_ml, s_xst, s_xe, s_xp = (
                sem(n) for n in ("s_xs", "s_xm", "s_xsum", "s_xlog", "s_shift", "s_mt", "s_mh", "s_ml", "s_xst",
                                 "s_xe", "s_xp"))
            s_x2 = sem("s_x2")
            s_f3p, s_f3, s_lg, s_top, s_esc, s_oh1, s_rank, s_pos, s_xr3, c_fin = (
                sem(n) for n in ("s_f3p", "s_f3", "s_lg", "s_top", "s_esc", "s_oh1", "s_rank", "s_pos", "s_xr3", "c_fin"))

            NSTAGE = 5
            whi = [wqh[:].rearrange("p k n -> p (k n)")[:, i * 2048:(i + 1) * 2048] for i in range(3)] + [
                woh[:].rearrange("p k n -> p (k n)")[:, i * 2048:(i + 1) * 2048] for i in range(2)]
            wlo = [wql[:].rearrange("p k n -> p (k n)")[:, i * 2048:(i + 1) * 2048] for i in range(3)] + [
                wol[:].rearrange("p k n -> p (k n)")[:, i * 2048:(i + 1) * 2048] for i in range(2)]
            wsrc = [A["wqkv"][:, i * 2048:(i + 1) * 2048] for i in range(3)] + [
                A["wo"][:, i * 2048:(i + 1) * 2048] for i in range(2)]

            SLOTS = 18
            COL = [NH * HD] + [512 * i for i in range(4)] + [(NH + NKV) * HD]

            PT_AT, PV_AT, OUT_AT = [9, 10, 12, 13], [10, 11, 13, 14], [11, 12, 14, 15]
            X_MAX, X_EXP = XH // 2, XH // 2 + 1
            SETV = 10

            def last(tile):
                return isinstance(tile[0], int) and num(tile) + 1 >= NT

            def tiles(eng, body):
                def peeled(t):
                    body((t // 2, t % 2), t < NT, 1 <= t <= NT, 2 <= t < NT + 2, 3 <= t < NT + 3)

                for t in range(FIRST):
                    peeled(t)
                if LAST > FIRST:
                    with eng.Fori(FIRST // 2, LAST // 2) as h:
                        body((h, 0), True, True, True, True)
                        body((h, 1), True, True, True, True)
                for t in range(max(LAST, FIRST), NT + 3):
                    peeled(t)

            block = pa.enter_context(nc.Block())

            @block.sync
            def _(sp):
                sp.dma_start(const[:], A["const"]).then_inc(s_const, 16)
                for p in range(2):
                    sp.dma_start(x[p][:], A["x"][p * P:(p + 1) * P, :]).then_inc(s_x[p], 16)
                for i in range(NSTAGE):
                    if i >= 2:
                        sp.wait_ge(s_lo, i - 1)
                        sp.wait_ge(s_hi, i - 1)
                    sp.dma_start(stage[:, i % 2, :], wsrc[i]).then_inc(s_stage[i % 2], 16)
                    if i == 0:
                        sp.dma_start(brow[:, 0:3072], A["bqkv"].partition_broadcast(P)).then_inc(s_bias, 16)
                        sp.dma_start(brow[:, 3072:], A["bo"].partition_broadcast(P)).then_inc(s_bias, 16)
                        sp.dma_start(sinks[:].rearrange("p r s -> p (r s)"),
                                     A["sinks"].partition_broadcast(P)).then_inc(s_bias, 16)
                        sp.dma_start(rw[:].rearrange("p k e -> p (k e)"), A["rw"]).then_inc(s_bias, 16)
                sp.wait_ge(s_setg, 1)
                for n in range(NRT - NT):
                    sp.dma_start(xg_d[DUMMY + n * P:DUMMY + (n + 1) * P, :], zeros[:]).then_inc(s_zero, 16)

                def body(tile, mha, prep, xatt, fin):
                    h, p = tile
                    t = num(tile)
                    if mha:
                        need(sp, s_cTp, t - 1)
                        need(sp, s_chl, t - 1)
                        sp.dma_start(ctx[p][:], A["ctx"][bass.ds(t * P, P), :]).then_inc(s_ctx[p], 16)
                    if prep:
                        s = back(tile, 1)
                        hs, ps = s
                        sp.wait_ge(s_chl, num(s) + 1)
                        for k, part in enumerate((0, 1, 0)):
                            sp.dma_start(stackk_d[ps][:, k], chl[:, part, :].bitcast(F32)).then_inc(s_stw[ps], 16)
                        sp.wait_ge(s_q2hl, num(s) + 1)
                        for k, part in enumerate((0, 0, 1)):
                            sp.dma_start(stackq_d[ps][:, k], q2hl[:, part, :].bitcast(F32)).then_inc(s_stw[ps], 16)
                        sp.wait_ge(s_stw[ps], (hs + 1) * 96)
                        for st, sd in ((stk[ps], stackk_d[ps]), (stq[ps], stackq_d[ps])):
                            v = sd.rearrange("(j g) s d m -> g (s d) j m", g=4)
                            for g in range(4):
                                sp.dma_start(st[32 * g:32 * g + 24].bitcast(F32), v[g]).then_inc(s_str[ps], 16)
                    if fin:
                        s = back(tile, 3)
                        sp.wait_ge(s_norm[2], num(s) + 1)
                        sp.dma_start(xn3_d[bass.ds(num(s) * P, P), :], xn3[s[1]][:]).then_inc(s_fst[s[1]], 16)
                        sp.dma_start(x2_d[bass.ds(num(s) * P, P), :], x2[s[1]][:]).then_inc(s_fst[s[1]], 16)
                    if mha:
                        sp.wait_ge(s_x1, t + 1)
                    if mha and not (isinstance(t, int) and t + 2 >= NT):
                        sp.dma_start(x[p][:], A["x"][bass.ds(t * P + 2 * P, P), :]).then_inc(s_x[p], 16)

                tiles(sp, body)
                for p in range(2):
                    sp.wait_ge(s_fst[p], 32 * (NT // 2))
                    sp.wait_ge(s_scat[p], 16 * (NT // 2))
                sp.wait_ge(s_zero, 16 * (NRT - NT))

            @block.gpsimd
            def _(pool):
                nc.gpsimd.memset(zeros[:], 0.0).then_inc(s_setg, 1)
                nc.gpsimd.memset(half_neg[:], -0.5)
                nc.gpsimd.memset(onesf[:], 1.0)
                nc.gpsimd.memset(onesb[:], 1.0)
                nc.gpsimd.memset(cT[:], 0.0)
                nc.gpsimd.memset(vbd[0][:], 0.0)
                nc.gpsimd.memset(vbd[1][:], 0.0).then_inc(s_setg, 1)
                pool.wait_ge(s_setg, 2)

                def settle(tile):
                    if in_loop(tile):
                        nc.gpsimd.tensor_tensor(spare_g[:], half_neg[:], half_neg[:], ALU.mult)

                def rsqrt(n, tile):
                    pool.wait_ge(s_var[n], num(tile) + 1)
                    need(pool, s_norm[n], num(tile))
                    settle(tile)
                    ch = Chain(pool, g_ln[n], 2 if n == 1 else 1, tile)
                    ch(nc.gpsimd.tensor_scalar(rstd[:, n, 1:2], mv[:, n, 1:2], EPS, None, ALU.add))
                    if n == 1:
                        ch(nc.gpsimd.tensor_tensor(rstd[:, n, 1:2], rstd[:, n, 1:2], half_neg[:], ALU.pow))
                        settle(tile)
                        nc.gpsimd.tensor_scalar(rstd[:, n, 0:1], rstd[:, n, 1:2], XD ** -0.5, None,
                                                ALU.mult).then_inc(s_rstd[n], 1)
                    else:
                        nc.gpsimd.tensor_tensor(rstd[:, n, 0:1], rstd[:, n, 1:2], half_neg[:],
                                                ALU.pow).then_inc(s_rstd[n], 1)
                    ch.end()

                def split(tile, src, hl, done, chain):
                    hb, pb = back(tile, 1)
                    need(pool, s_stw[pb], (hb + 1) * 96)
                    settle(tile)
                    ch = Chain(pool, chain, 1, tile)
                    ch(nc.gpsimd.tensor_copy(hl[:, 0, :], src))
                    nc.gpsimd.tensor_tensor(hl[:, 1, :], src, hl[:, 0, :].bitcast(F32),
                                            ALU.subtract).then_inc(done, 1)
                    ch.end()

                def norm_probs(tile, r):
                    pool.wait_ge(s_rden, num(tile) * 2 + r + 1)
                    v = prob[:, r, 0:16 * HD].rearrange("p (h k) -> p h k", k=HD)
                    nc.gpsimd.tensor_tensor(v, v, rden[:, r, :].unsqueeze(2).to_broadcast([P, 16, HD]),
                                            ALU.mult).then_inc(s_pn, 1)

                def body(tile, mha, prep, xatt, fin):
                    t = num(tile)
                    s1, s3 = back(tile, 1), back(tile, 3)
                    if prep:
                        pool.wait_ge(s_ctx[s1[1]], (s1[0] + 1) * 16)
                        split(s1, ctx[s1[1]][:], chl, s_chl, g_c)
                    if fin:
                        rsqrt(2, s3)
                    if prep:
                        rsqrt(1, s1)
                        pool.wait_ge(s_norm[1], num(s1) + 1)
                        split(s1, q2[:], q2hl, s_q2hl, g_q2)
                    if mha and not last(tile):
                        rsqrt(0, ahead(tile))
                    if mha:
                        norm_probs(tile, 0)
                    if fin:
                        pool.wait_ge(s_pos, num(s3) + 1)
                        pool.wait_ge(s_xr3, num(s3) + 1)
                        nc.gpsimd.indirect_dma_start(
                            out=xg_d, out_offset=bass.IndirectOffsetOnAxis(ap=posx[s3[1]][:, 0:1], axis=0),
                            in_=xr[s3[1]][:], in_offset=None,
                            bounds_check=num(s3) + XROWS).then_inc(s_scat[s3[1]], 16)
                    if mha:
                        norm_probs(tile, 1)

                rsqrt(0, (0, 0))
                tiles(pool, body)

            @block.scalar
            def _(act):
                for i in range(NSTAGE):
                    act.wait_ge(s_stage[i % 2], 16 * (i // 2 + 1))
                    nc.scalar.activation(whi[i], stage[:, i % 2, :], ACT.Copy).then_inc(s_hi, 1)

                def turn_norm(tile):
                    act.wait_ge(s_xnTp, num(tile) + 1)
                    nc.scalar.activation(xnTh[:], b4[:, 0, 0:D].rearrange("p (k n) -> p k n", k=2),
                                         ACT.Copy).then_inc(s_xnTh, 1)

                def evac_qk(tile, n):
                    t = num(tile)
                    act.wait_ge(s_turn, t * 5 + n + 1)
                    if n == 0:
                        need(act, s_S, t * 2)
                    dst = kT[:] if n == 0 else qT[:, 4 * (n - 1):4 * n, :]
                    nc.scalar.activation(dst, bS[:, n % 2, :].rearrange("p (a b) -> p a b", a=4),
                                         ACT.Copy).then_inc(s_qkT, 1)

                def evac_v(tile):
                    t = num(tile)
                    act.wait_ge(s_qkv, t * 6 + 6)
                    need(act, s_pv, t * 4)
                    v = bk[1][:, 0, :].rearrange("p (a o d) -> p o a d", o=2, d=HD)
                    for b in range(2):
                        for o in range(2):
                            ins = nc.scalar.activation(vbd[b][o * HD:(o + 1) * HD, :, o * HD:(o + 1) * HD],
                                                       v[b * T:(b + 1) * T, o], ACT.Copy)
                    ins.then_inc(s_v, 1)

                def exp_probs(tile, r):
                    act.wait_ge(s_sub, num(tile) * 2 + r + 1)
                    v = prob[:, r]
                    nc.scalar.activation(v, v, ACT.Exp).then_inc(s_exp, 1)

                def evac_PT(tile, g):
                    t = num(tile)
                    act.wait_ge(s_PTp, t * 4 + g + 1)
                    need(act, s_pv, t * 4 + g - 1)
                    nc.scalar.activation(probT[g % 2][:], bk[0][:, 0, :].rearrange("p (a b) -> p a b", a=4),
                                         ACT.Copy).then_inc(s_PT, 1)

                def evac_O(tile, g):
                    t = num(tile)
                    act.wait_ge(s_pv, t * 4 + g + 1)
                    need(act, s_out, t * 4 + g - 1)
                    nc.scalar.activation(oTh[g % 2][:], bk[1][:, 0, :].rearrange("p (a b) -> p a b", a=4),
                                         ACT.Copy).then_inc(s_oh, 1)

                def evac_ctx(s):
                    act.wait_ge(s_cTp, num(s) + 1)
                    need(act, s_xp, num(s) * XH)
                    nc.scalar.activation(cT[:, :, :, 0:XD], b7[:, 0, 0:D].rearrange("p (k h c) -> p k h c", k=2, c=XD),
                                         ACT.Copy).then_inc(s_cT, 1)

                def sum_x(s, hd):
                    act.wait_ge(s_xm, num(s) * XH + hd + 1)
                    if hd == 0:
                        need(act, s_xlog, num(s))
                    for m in range(2):
                        v = bX[:, hd % 2, m * D:(m + 1) * D]
                        ins = nc.scalar.activation(v, v, ACT.Exp,
                                                   bias=xmax[:, m, hd:hd + 1], accum_out=xsum[:, m, hd:hd + 1])
                    ins.then_inc(s_xsum, 1)

                def log_x(s):
                    act.wait_ge(s_xsum, (num(s) + 1) * XH)
                    need(act, s_shift, num(s))
                    nc.scalar.activation(xlog[:], xsum[:], ACT.Ln).then_inc(s_xlog, 1)

                def evac_max(s):
                    act.wait_ge(s_mt, num(s) + 1)
                    need(act, s_xst, num(s) * XH)
                    nc.scalar.activation(xmaxT[0:XH, :], b7[0:XH, 0, D:2 * D], ACT.Copy).then_inc(s_mh, 1)

                def exp_x(s, hd):
                    act.wait_ge(s_xst, num(s) * XH + hd + 1)
                    need(act, s_xp, num(s) * XH + hd - 1)
                    nc.scalar.activation(xe[hd % 2][:].rearrange("p n m -> p (n m)"), bX[:, hd % 2, :],
                                         ACT.Exp).then_inc(s_xe, 1)

                def body(tile, mha, prep, xatt, fin):
                    s2, s3 = back(tile, 2), back(tile, 3)
                    if xatt:
                        evac_ctx(s2)
                    for k in range(SLOTS):
                        if fin and k == 2:
                            act.wait_ge(s_f3p, num(s3) + 1)
                            nc.scalar.activation(xn3T[:], b4[:, 0, 0:D].rearrange("p (k n) -> p k n", k=2),
                                                 ACT.Copy).then_inc(s_f3, 1)
                        if fin and k == 4:
                            act.wait_ge(c_fin, num(s3) * 8 + 1)
                            nc.scalar.activation(score[:, 0:1], top8[:, 0:1], ACT.Exp, scale=-1.0).then_inc(s_esc, 1)
                        if mha and 1 <= k <= 5:
                            evac_qk(tile, k - 1)
                        if mha and k == 5:
                            evac_v(tile)
                        if mha and k in (7, 9):
                            exp_probs(tile, (k - 7) // 2)
                        if mha and k == 8 and not last(tile):
                            turn_norm(ahead(tile))
                        if mha and k in PV_AT:
                            evac_O(tile, PV_AT.index(k))
                        if mha and k in PT_AT:
                            evac_PT(tile, PT_AT.index(k))
                        if xatt and k < XH // 2:
                            sum_x(s2, 2 * k)
                            sum_x(s2, 2 * k + 1)
                        if xatt and k == X_MAX - 1:
                            log_x(s2)
                        if xatt and k == X_MAX:
                            evac_max(s2)
                        if xatt and X_EXP <= k < X_EXP + XH // 2:
                            exp_x(s2, 2 * (k - X_EXP))
                            exp_x(s2, 2 * (k - X_EXP) + 1)

                turn_norm((0, 0))
                tiles(act, body)

            @block.vector
            def _(dve):
                dve.wait_ge(s_const, 16)
                dve.wait_ge(s_setg, 2)
                nc.vector.tensor_copy(identb[:], ident)
                nc.vector.tensor_copy(maskb[:], C["mask"])
                nc.vector.tensor_copy(selh[:], C["sel"][0:MR].unsqueeze(2).to_broadcast([MR, XH, P]))
                nc.vector.tensor_copy(xmaxT[:], onesf[0:MR, 0:1].to_broadcast([MR, D]))
                nc.vector.tensor_copy(run[:], C["base"]).then_inc(s_setv, 1)

                dve.wait_ge(s_bias, 64)
                n = 1
                for k in range(3):
                    sel = C["rowsel"][:, k:k + 1]
                    nc.vector.tensor_copy(btmp[:], brow[:]).then_inc(s_setv, 1)
                    n += 1
                    dve.wait_ge(s_setv, n)
                    if k == 0:
                        nc.vector.tensor_scalar(bias3[:], btmp[:], sel, None, ALU.mult).then_inc(s_setv, 1)
                    else:
                        nc.vector.scalar_tensor_tensor(bias3[:], btmp[:], sel, bias3[:], ALU.mult,
                                                       ALU.add).then_inc(s_setv, 1)
                    nc.vector.tensor_tensor(brow[:], brow[:], btmp[:], ALU.subtract).then_inc(s_setv, 1)
                    n += 2
                    dve.wait_ge(s_setv, n)
                assert n == SETV
                for i in range(NSTAGE):
                    dve.wait_ge(s_hi, i + 1)
                    nc.vector.tensor_tensor(wlo[i], stage[:, i % 2, :], whi[i].bitcast(F32),
                                            ALU.subtract).then_inc(s_lo, 1)

                def settle(tile):
                    if in_loop(tile):
                        nc.vector.memset(spare_v[:], 0.0)

                def stats_of(n, tile, src):
                    ch = Chain(dve, c_ln[n], 1, tile)
                    ch(nc.vector.bn_stats(stats[:, n, :], src))
                    settle(tile)
                    nc.vector.bn_aggr(mv[:, n, :], stats[:, n, :]).then_inc(s_var[n], 1)

                def normalise(n, tile, out, src):
                    dve.wait_ge(s_rstd[n], num(tile) + 1)
                    nc.vector.tensor_scalar(out, src, mv[:, n, 0:1], rstd[:, n, 0:1], ALU.subtract,
                                            ALU.mult).then_inc(s_norm[n], 1)

                def stats1(tile):
                    dve.wait_ge(s_x[tile[1]], (tile[0] + 1) * 16)
                    stats_of(0, tile, x[tile[1]][:])

                def norm1(tile):
                    need(dve, s_xnTp, num(tile))
                    normalise(0, tile, xn[:], x[tile[1]][:])

                def turn_rest(tile):
                    dve.wait_ge(s_xnTh, num(tile) + 1)
                    nc.vector.tensor_tensor(xnTl[:], b4[:, 0, 0:D].rearrange("p (k n) -> p k n", k=2),
                                            xnTh[:].bitcast(F32), ALU.subtract).then_inc(s_xnT, 1)

                def rope(tile, c):
                    t = num(tile)
                    dve.wait_ge(s_qkv, t * 6 + c + 1)
                    need(dve, s_turn, t * 5 + max(c - 1, 0))
                    cos, sin = (C["cosk"], C["sink"]) if c == 0 else (C["cosq"], C["sinq"])
                    src = bk[c % 2][:, 0, :].rearrange("p (h d) -> p h d", d=HD)
                    half = HD // 2
                    nc.vector.tensor_tensor(ropeC[c % 2][:].rearrange("p (h d) -> p h d", d=HD), src,
                                            cos.unsqueeze(1).to_broadcast([P, 8, HD]), ALU.mult)
                    out = ropeD[c % 2][:].rearrange("p (h d) -> p h d", d=HD)
                    nc.vector.tensor_tensor(out[:, :, 0:half], src[:, :, half:HD],
                                            sin[:, 0:half].unsqueeze(1).to_broadcast([P, 8, half]), ALU.mult)
                    nc.vector.tensor_tensor(out[:, :, half:HD], src[:, :, 0:half],
                                            sin[:, half:HD].unsqueeze(1).to_broadcast([P, 8, half]),
                                            ALU.mult).then_inc(s_rope, 1)

                def shift(tile, r, ch):
                    t = num(tile)
                    dve.wait_ge(s_S, t * 2 + r + 1)
                    need(dve, s_PTp, (t - 1) * 4 + 2 * (r + 1))
                    sc = bS[:].rearrange("p o (j k) -> p o j k", k=HD)
                    ch(nc.vector.tensor_reduce(mx[:, r, :], sc, AX.X, ALU.max))
                    m = mx[:, r, :].rearrange("p (o j) -> p o j", o=2)
                    nc.vector.tensor_tensor(prob[:, r, 16 * HD:].rearrange("p (j o) -> p o j", o=2),
                                            sinks[:, r, :].rearrange("p (o j) -> p o j", o=2), m, ALU.subtract)
                    nc.vector.tensor_tensor(prob[:, r, 0:16 * HD].rearrange("p (j o k) -> p o j k", o=2, k=HD), sc,
                                            m.unsqueeze(3).to_broadcast([P, 2, 8, HD]),
                                            ALU.subtract).then_inc(s_sub, 1)

                def denominator(tile, r, ch):
                    t = num(tile)
                    dve.wait_ge(s_exp, t * 2 + r + 1)
                    need(dve, s_pn, (t - 1) * 2 + r + 1)
                    ch(nc.vector.tensor_reduce(den[:, r, :], prob[:, r, 0:16 * HD].rearrange("p (h k) -> p h k", k=HD),
                                               AX.X, ALU.add))
                    ch(nc.vector.tensor_tensor(dsum[:, r, :], den[:, r, :], prob[:, r, 16 * HD:], ALU.add))
                    nc.vector.reciprocal(rden[:, r, :], dsum[:, r, :]).then_inc(s_rden, 1)

                def rest_O(tile, g):
                    t = num(tile)
                    dve.wait_ge(s_oh, t * 4 + g + 1)
                    nc.vector.tensor_tensor(oTl[g % 2][:], bk[1][:, 0, :].rearrange("p (a b) -> p a b", a=4),
                                            oTh[g % 2][:].bitcast(F32), ALU.subtract).then_inc(s_o, 1)

                def max_x(s, hd):
                    dve.wait_ge(s_xs, num(s) * XH + hd + 1)
                    if hd == 0:
                        need(dve, s_shift, num(s))
                    nc.vector.tensor_reduce(xmax[:, :, hd], bX[:, hd % 2, :].rearrange("p (m n) -> p m n", m=2),
                                            AX.X, ALU.max, negate=True).then_inc(s_xm, 1)

                def shift_x(s):
                    dve.wait_ge(s_xlog, num(s) + 1)
                    need(dve, s_mt, num(s))
                    nc.vector.tensor_tensor(xshift[:], xmax[:], xlog[:], ALU.subtract).then_inc(s_shift, 1)

                def rest_max(s):
                    dve.wait_ge(s_mh, num(s) + 1)
                    nc.vector.tensor_tensor(xmaxT[32:MR, :], b7[0:XH, 0, D:2 * D], xmaxT[0:XH, :].bitcast(F32),
                                            ALU.subtract).then_inc(s_ml, 1)

                def finish_x(s, p):
                    dve.wait_ge(s_xp, (num(s) + 1) * XH)
                    need(dve, s_fst[p], s[0] * 32)
                    nc.vector.tensor_tensor(x2[p][:], x1[p][:], b7[:, 0, 0:D], ALU.add).then_inc(s_x2, 1)

                def choose(s, ch):
                    dve.wait_ge(s_lg, num(s) + 1)
                    lg = b4[:, 0, D:D + E]
                    settle(s)
                    ch(nc.vector.max(top8[:], lg))
                    settle(s)
                    ch(nc.vector.max_index(idx8[:], top8[:], lg))
                    ch(nc.vector.tensor_copy(idxf[:], idx8[:, 0:1]))
                    nc.vector.tensor_scalar(onehot[:], C["iota8"], idxf[:, 0:1], None, ALU.is_equal).then_inc(s_oh1, 1)

                def place(s, ch):
                    p = s[1]
                    dve.wait_ge(s_rank, num(s) + 1)
                    need(dve, s_scat[p], s[0] * 16)
                    ch(nc.vector.tensor_tensor(pos8[:], b4[:, 0, D + 8:D + 16], run[:], ALU.add))
                    ch(nc.vector.tensor_tensor_reduce(out=ptmp[:], in0=pos8[:], in1=onehot[:], scale=1.0, scalar=0.0,
                                                      op0=ALU.mult, op1=ALU.add, accum_out=posf[:]))
                    ch(nc.vector.tensor_tensor(run[:], run[:], b4[:, 0, D + 16:D + 24], ALU.add))
                    nc.vector.tensor_copy(posall[:, bass.ds(num(s), 1)], posf[:])
                    nc.vector.tensor_copy(posx[p][:], posf[:]).then_inc(s_pos, 1)
                    dve.wait_ge(s_esc, num(s) + 1)
                    ch(nc.vector.tensor_scalar(score[:, 1:2], score[:, 0:1], 1.0, None, ALU.add))
                    ch(nc.vector.reciprocal(score[:, 2:3], score[:, 1:2]))
                    nc.vector.tensor_scalar(xr[p][:], xn3[p][:], score[:, 2:3], None, ALU.mult).then_inc(s_xr3, 1)

                def body(tile, mha, prep, xatt, fin):
                    t = num(tile)
                    p = tile[1]
                    s1, s2, s3 = back(tile, 1), back(tile, 2), back(tile, 3)
                    soft = Chain(dve, c_soft, 6, tile)
                    routing = Chain(dve, c_fin, 8, s3)
                    for k in range(SLOTS):
                        if k == 0:
                            if fin:
                                dve.wait_ge(s_x2, num(s3) + 1)
                                stats_of(2, s3, x2[s3[1]][:])
                            if prep:
                                dve.wait_ge(s_x1, num(s1) + 1)
                                stats_of(1, s1, x1[s1[1]][:])
                        if mha:
                            if k == 0:
                                rope(tile, 0)
                            if k <= 3:
                                rope(tile, k + 1)
                            if k == 8:
                                denominator(tile, 0, soft)
                                if not last(tile):
                                    turn_rest(ahead(tile))
                            if k == 6:
                                shift(tile, 0, soft)
                            if k == 8:
                                shift(tile, 1, soft)
                            if k == 10:
                                denominator(tile, 1, soft)
                            if k in PV_AT:
                                rest_O(tile, PV_AT.index(k))
                        if k == 1:
                            if fin:
                                need(dve, s_fst[s3[1]], s3[0] * 32)
                                normalise(2, s3, xn3[s3[1]][:], x2[s3[1]][:])
                            if prep:
                                need(dve, s_q2hl, num(s1))
                                normalise(1, s1, q2[:], x1[s1[1]][:])
                        if mha and k == 4 and not last(tile):
                            stats1(ahead(tile))
                        if mha and k == 5 and not last(tile):
                            norm1(ahead(tile))
                        if fin and k == 3:
                            choose(s3, routing)
                        if fin and k == 6:
                            place(s3, routing)
                        if xatt and k < XH // 2:
                            max_x(s2, 2 * k)
                            max_x(s2, 2 * k + 1)
                        if xatt and k == X_MAX - 1:
                            shift_x(s2)
                        if xatt and k == X_MAX:
                            rest_max(s2)
                    if xatt:
                        finish_x(s2, p)
                    if mha:
                        if xatt:
                            dve.wait_ge(s_x2, num(s2) + 1)
                        dve.wait_ge(s_out, (t + 1) * 4)
                        nc.vector.tensor_tensor(x1[p][:], x[p][:], b4[:, 0, 0:D], ALU.add).then_inc(s_x1, 1)

                stats1((0, 0))
                norm1((0, 0))
                turn_rest((0, 0))
                tiles(dve, body)

            @block.tensor
            def _(pe):
                pe.wait_ge(s_const, 16)
                pe.wait_ge(s_setg, 2)

                def turn(out, src, first=True, final=True):
                    return nc.tensor.matmul(out, src, ident, is_transpose=True, start=first, stop=final)

                def turn_norm(tile):
                    pe.wait_ge(s_norm[0], num(tile) + 1)
                    need(pe, s_pos, num(tile) - 3)
                    for k in range(2):
                        ins = turn(b4[:, 0, k * P:(k + 1) * P], xn[:, k * P:(k + 1) * P])
                    ins.then_inc(s_xnTp, 1)

                def project(tile, c):
                    t = num(tile)
                    if c == 0:
                        pe.wait_ge(s_xnT, t + 1)
                        need(pe, s_PT, t * 4)
                    elif c == 1:
                        need(pe, s_o, t * 4)
                    else:
                        pe.wait_ge(s_rope, t * 5 + c - 1)
                    out, col = bk[c % 2][:, 0, :], COL[c]
                    nc.tensor.matmul(out, onesb[:], bias3[:, col:col + 512], start=True, stop=False)
                    for k in range(2):
                        for n, (a, w) in enumerate(((xnTh, wqh), (xnTh, wql), (xnTl, wqh))):
                            ins = nc.tensor.matmul(out, a[:, k, :], w[:, k, col:col + 512], start=False,
                                                   stop=(k == 1 and n == 2))
                    ins.then_inc(s_qkv, 1)

                def turn_qk(tile, n):
                    t = num(tile)
                    pe.wait_ge(s_rope, t * 5 + n + 1)
                    if n < 2:
                        need(pe, s_sub, t * 2)
                    else:
                        pe.wait_ge(s_qkT, t * 5 + n - 1)
                    for j in range(4):
                        for i, r in enumerate((ropeC[n % 2], ropeD[n % 2])):
                            ins = turn(bS[:, n % 2, j * P:(j + 1) * P], r[:, j * P:(j + 1) * P], i == 0, i == 1)
                    ins.then_inc(s_turn, 1)

                def scores(tile, r):
                    t = num(tile)
                    if r == 0:
                        pe.wait_ge(s_qkT, t * 5 + 5)
                    else:
                        pe.wait_ge(s_sub, t * 2 + 1)
                    for o in range(2):
                        nc.tensor.matmul(bS[:, o, :], identb[:], maskb[:], start=True, stop=False,
                                         skip_group_check=True)
                    for j in range(8):
                        for b in range(2):
                            for o in range(2):
                                ins = nc.tensor.matmul(
                                    bS[b * T:(b + 1) * T, o, j * HD:(j + 1) * HD],
                                    qT[o * HD:(o + 1) * HD, 8 * r + j, b * T:(b + 1) * T],
                                    kT[o * HD:(o + 1) * HD, (8 * r + j) // 4, b * T:(b + 1) * T],
                                    start=False, stop=True, skip_group_check=True)
                    ins.then_inc(s_S, 1)

                def turn_probs(tile, g):
                    t = num(tile)
                    pe.wait_ge(s_pn, t * 2 + g // 2 + 1)
                    if g == 0:
                        pe.wait_ge(s_rope, t * 5 + 5)
                    else:
                        pe.wait_ge(s_PT, t * 4 + g)
                    for j in range(4):
                        at = (4 * (g % 2) + j) * P
                        ins = turn(bk[0][:, 0, j * P:(j + 1) * P], prob[:, g // 2, at:at + P])
                    ins.then_inc(s_PTp, 1)

                def results(tile, g):
                    t = num(tile)
                    pe.wait_ge(s_PT, t * 4 + g + 1)
                    if g == 0:
                        pe.wait_ge(s_v, t + 1)
                    else:
                        pe.wait_ge(s_o, t * 4 + g)
                    out = bk[1][:, 0, :].rearrange("p (j b q) -> p j b q", j=4, b=2)
                    src = probT[g % 2][:].rearrange("p j (b q) -> p j b q", b=2)
                    for b in range(2):
                        ins = nc.tensor.matmul(out[:, :, b, :], vbd[b][:, g, :], src[:, :, b, :], start=True, stop=True)
                    ins.then_inc(s_pv, 1)

                def project_out(tile, g):
                    t = num(tile)
                    pe.wait_ge(s_o, t * 4 + g + 1)
                    out = b4[:, 0, 0:D]
                    if g == 0:
                        if last(tile):
                            need(pe, s_pos, t - 2)
                        else:
                            pe.wait_ge(s_xnT, t + 2)
                        nc.tensor.matmul(out, onesb[:], bias3[:, 3072:3072 + D], start=True, stop=False)
                    for j in range(4):
                        for n, (a, w) in enumerate(((oTh, woh), (oTh, wol), (oTl, woh))):
                            ins = nc.tensor.matmul(out, a[g % 2][:, j, :], w[:, 4 * g + j, :], start=False,
                                                   stop=(g == 3 and j == 3 and n == 2))
                    ins.then_inc(s_out, 1)

                def turn_ctx(s, p):
                    need(pe, s_x2, num(s))
                    for k in range(2):
                        ins = turn(b7[:, 0, k * P:(k + 1) * P], ctx[p][:, k * P:(k + 1) * P])
                    ins.then_inc(s_cTp, 1)

                def scores_x(s, hd):
                    h, p = s
                    if hd == 0:
                        pe.wait_ge(s_str[p], (h + 1) * 128)
                    if hd < 2:
                        need(pe, s_xe, (num(s) - 1) * XH + XH + hd - 1)
                    else:
                        pe.wait_ge(s_xsum, num(s) * XH + hd - 1)
                    g, j = hd % 4, hd // 4
                    for m in range(2):
                        ins = nc.tensor.matmul(bX[:, hd % 2, m * D:(m + 1) * D],
                                               stq[p][32 * g:32 * g + 24, j, m * P:(m + 1) * P],
                                               stk[p][32 * g:32 * g + 24, j, :], start=True, stop=True)
                    ins.then_inc(s_xs, 1)

                def turn_max(s):
                    pe.wait_ge(s_shift, num(s) + 1)
                    for m in range(2):
                        ins = turn(b7[0:XH, 0, D + m * P:D + (m + 1) * P], xshift[:, m, :])
                    ins.then_inc(s_mt, 1)

                def turned_scores_x(s, hd):
                    p = s[1]
                    if hd == 0:
                        pe.wait_ge(s_ml, num(s) + 1)
                    if hd >= 2:
                        pe.wait_ge(s_xe, num(s) * XH + hd - 1)
                    g, j = hd % 4, hd // 4
                    out = bX[:, hd % 2, :]
                    for n in range(2):
                        nc.tensor.matmul(out[:, n * D:(n + 1) * D], selh[:, hd, :], xmaxT[:], start=(n == 0), stop=False,
                                         skip_group_check=True)
                    for n in range(2):
                        ins = nc.tensor.matmul(out[:, n * D:(n + 1) * D],
                                               stk[p][32 * g:32 * g + 24, j, n * P:(n + 1) * P],
                                               stq[p][32 * g:32 * g + 24, j, :], start=False, stop=True,
                                               skip_group_check=True)
                    ins.then_inc(s_xst, 1)

                cTf = cT[:].rearrange("p k h c -> p k (h c)")

                def results_x(s, hd):
                    pe.wait_ge(s_xe, num(s) * XH + hd + 1)
                    if hd == 0:
                        pe.wait_ge(s_cT, num(s) + 1)
                    for n in range(2):
                        ins = nc.tensor.matmul(b7[:, 0, 0:D], cTf[:, n, hd * P:(hd + 1) * P], xe[hd % 2][:, n, :],
                                               start=(hd == 0 and n == 0), stop=(hd == XH - 1 and n == 1),
                                               skip_group_check=True)
                    ins.then_inc(s_xp, 1)

                def route(s, k):
                    if k == 2:
                        pe.wait_ge(s_norm[2], num(s) + 1)
                        need(pe, s_x1, min(num(s) + 3, NT) if isinstance(s[0], int) else num(s) + 3)
                        for i in range(2):
                            ins = turn(b4[:, 0, i * P:(i + 1) * P], xn3[s[1]][:, i * P:(i + 1) * P])
                        ins.then_inc(s_f3p, 1)
                    if k == 3:
                        pe.wait_ge(s_f3, num(s) + 1)
                        for i in range(2):
                            ins = nc.tensor.matmul(b4[:, 0, D:D + E], xn3T[:, i, :], rw[:, i, :], start=(i == 0),
                                                   stop=(i == 1))
                        ins.then_inc(s_lg, 1)
                    if k == 5:
                        pe.wait_ge(s_oh1, num(s) + 1)
                        nc.tensor.matmul(b4[:, 0, D + 8:D + 16], C["tri"], onehot[:], start=True, stop=True)
                        nc.tensor.matmul(b4[:, 0, D + 16:D + 24], onesf[:], onehot[:], start=True,
                                         stop=True).then_inc(s_rank, 1)

                def body(tile, mha, prep, xatt, fin):
                    t = num(tile)
                    s2, s3 = back(tile, 2), back(tile, 3)
                    if xatt:
                        turn_ctx(s2, tile[1])
                    for k in range(SLOTS):
                        if mha:
                            if k == 0:
                                project(tile, 0)
                            if 1 <= k <= 5:
                                turn_qk(tile, k - 1)
                            if k in (6, 8):
                                scores(tile, (k - 6) // 2)
                            if k in PV_AT:
                                results(tile, PV_AT.index(k))
                        if xatt and k == X_MAX:
                            turn_max(s2)
                        if mha:
                            if k <= 4:
                                project(tile, k + 1)
                            if k == 7 and not last(tile):
                                turn_norm(ahead(tile))
                            if k in PT_AT:
                                turn_probs(tile, PT_AT.index(k))
                            if k in OUT_AT:
                                project_out(tile, OUT_AT.index(k))
                        if fin:
                            route(s3, k)
                        if xatt:
                            for i in range(2):
                                hd = 2 * (k - X_EXP) + i
                                if k < XH // 2:
                                    scores_x(s2, 2 * k + i)
                                if 0 <= hd - 2 < XH:
                                    results_x(s2, hd - 2)
                                if 0 <= hd < XH:
                                    turned_scores_x(s2, hd)

                turn_norm((0, 0))
                pe.wait_ge(s_setv, SETV)
                pe.wait_ge(s_lo, NSTAGE)
                tiles(pe, body)

        with ExitStack() as pc:
            def sb(name, shape, dt=F32):
                return pc.enter_context(nc.sbuf_tensor(name, shape, dt))

            def sem(name):
                return pc.enter_context(nc.semaphore(name))

            wexp = sb("wexp", [P, (E + 1) * WE])
            cnt, ntile, cum, ones8, ge, lim, v0, bad, ptmp2 = (
                sb(n, [P, E]) for n in ("cnt", "ntile", "cum", "ones8", "ge", "lim", "v0", "bad", "ptmp2"))
            above = sb("above", [P, E, NT])
            moved = sb("moved", [P, E])
            past = sb("past", [P, NT, E])
            shift_y = sb("shift_y", [P, NT])
            yrow = sb("yrow", [P, NT])
            ei, si, dist = (sb(n, [P, 1]) for n in ("ei", "si", "dist"))
            tabf = sb("tabf", [P, 2])
            tabi = sb("tabi", [P, 2], I32)
            padi = sb("padi", [P, E], I32)
            padx = [sb(f"padx{e}", [P, 1], I32) for e in range(E)]
            tabr = sb("tabr", [1, 2 * P], I32)
            xin = [sb(f"xin{p}", [P, D]) for p in range(2)]
            xT = [sb(f"xT{p}", [P, 2, P]) for p in range(2)]
            gate = sb("gate", [P, FF])
            hid = [sb(f"hid{p}", [P, FF]) for p in range(2)]
            hT = sb("hT", [P, 4, P])
            y = [sb(f"y{p}", [P, D]) for p in range(2)]
            ysum = sb("ysum", [P, D])
            x2in = [sb(f"x2in{p}", [P, D]) for p in range(2)]
            gat = [sb(f"gat{p}", [P, D]) for p in range(2)]
            posc = [sb(f"posc{p}", [P, 1], I32) for p in range(2)]

            s_w, c_tab, s_yrow, s_tabi, s_tabd, s_tab, s_pad, s_padd = (
                sem(n) for n in ("s_w", "c_tab", "s_yrow", "s_tabi", "s_tabd", "s_tab", "s_pad", "s_padd"))
            s_xin, s_yst, s_x2in, s_gat = ([sem(f"{n}{p}") for p in range(2)] for n in ("s_xin", "s_yst", "s_x2in", "s_gat"))
            s_tx, s_xT, s_g, s_u, s_silu, s_h, s_th, s_hT, s_d, s_y, c_y, s_posc = (
                sem(n) for n in ("s_tx", "s_xT", "s_g", "s_u", "s_silu", "s_h", "s_th", "s_hT", "s_d", "s_y", "c_y", "s_posc"))

            def seq(eng, body, routed_to, shared_from):
                def run_to(a, b):
                    if b - a >= 4:
                        with eng.Fori(a // 2, b // 2) as h:
                            body((h, 0), a)
                            body((h, 1), a + 1)
                    else:
                        for n in range(a, b):
                            body((n // 2, n % 2), n)
                for n in range(2):
                    body((0, n), n)
                run_to(2, routed_to)
                for n in range(routed_to, shared_from):
                    body((n // 2, n % 2), n)
                end = NALL - 2
                run_to(shared_from, end)
                for n in range(end, NALL + 1):
                    body((n // 2, n % 2), n)

            block = pc.enter_context(nc.Block())

            @block.sync
            def _(sp):
                for e in range(E + 1):
                    sp.dma_start(wexp[:, e * WE:(e + 1) * WE], A["wexp"][e]).then_inc(s_w, 16)
                sp.wait_ge(s_tabi, 1)
                sp.dma_start(tab_d, tabi[:]).then_inc(s_tabd, 16)
                sp.wait_ge(s_tabd, 16)
                sp.dma_start(tabr[:], tab_d.rearrange("p (o c) -> o (p c)", o=1)).then_inc(s_tab, 16)
                sp.wait_ge(s_tab, 16)
                sp.wait_ge(s_padd, 16 * E)

                def row(tile):
                    return sp.value_load(tabr[0:1, bass.ds(num(tile) * 2, 1)], min_val=0, max_val=XROWS - P)

                def load(tile, like):
                    h, p = tile
                    need(sp, s_tx, num(tile) - 1)
                    if like < NRT:
                        src = xg_d[bass.ds(row(tile), P), :]
                    else:
                        src = xn3_d[bass.ds(num(tile) * P - NRT * P, P), :]
                    sp.dma_start(xin[p][:], src).then_inc(s_xin[p], 16)

                def load_residual(tile):
                    sp.wait_ge(s_y, num(tile) - 1)
                    sp.dma_start(x2in[tile[1]][:], x2_d[bass.ds(num(tile) * P - NRT * P, P), :]).then_inc(
                        s_x2in[tile[1]], 16)

                def store(tile, like):
                    h, p = tile
                    sp.wait_ge(s_y, num(tile) + 1)
                    if like < NRT:
                        sp.dma_start(yg_d[bass.ds(num(tile) * P, P), :], y[p][:]).then_inc(s_yst[p], 16)
                    else:
                        sp.dma_start(A["out"][bass.ds(num(tile) * P - NRT * P, P), :], y[p][:]).then_inc(s_yst[p], 16)

                def body(tile, n):
                    if n + 2 < NALL:
                        load((tile[0] + 1, tile[1]), n + 2)
                    if n >= 1:
                        store(back(tile, 1), n - 1)
                    if NRT <= n < NALL:
                        load_residual(tile)

                load((0, 0), 0)
                load((0, 1), 1)
                seq(sp, body, NRT - 2, NRT + 2)
                for p in range(2):
                    sp.wait_ge(s_yst[p], 16 * (NALL // 2))

            @block.gpsimd
            def _(pool):
                nc.gpsimd.memset(ones8[:], 1.0).then_inc(s_posc, 1)
                pool.wait_ge(s_pad, 1)
                for e in range(E):
                    nc.gpsimd.indirect_dma_start(
                        out=xg_d, out_offset=bass.IndirectOffsetOnAxis(ap=padx[e][:, 0:1], axis=0),
                        in_=zeros[:], in_offset=None, bounds_check=DUMMY - 1, oob_is_err=False).then_inc(s_padd, 16)
                pool.wait_ge(s_padd, 16 * E)
                pool.wait_ge(s_yrow, 1)
                for p in range(2):
                    pool.wait_ge(s_yst[p], 16 * (NRT // 2))

                def gather(tile):
                    h, p = tile
                    t = num(tile)
                    need(pool, s_gat[p], h * 16)
                    nc.gpsimd.tensor_copy(posc[p][:], yrow[:, bass.ds(t, 1)]).then_inc(s_posc, 1)
                    pool.wait_ge(s_y, t + NRT - 1)
                    pool.wait_ge(s_posc, t + 2)
                    nc.gpsimd.indirect_dma_start(
                        out=gat[p][:], out_offset=None, in_=yg_d,
                        in_offset=bass.IndirectOffsetOnAxis(ap=posc[p][:, 0:1], axis=0),
                        bounds_check=t + XROWS).then_inc(s_gat[p], 16)

                with pool.Fori(0, NT // 2) as h:
                    gather((h, 0))
                    gather((h, 1))

            @block.scalar
            def _(act):
                def body(tile, n):
                    t, p = num(tile), tile[1]
                    if n < NALL:
                        act.wait_ge(s_g, t + 1)
                        need(act, s_h, t)
                        nc.scalar.activation(gate[:], bk[p][:, 0, :], ACT.Silu).then_inc(s_silu, 1)
                    if n >= 1:
                        act.wait_ge(s_th, t)
                        need(act, s_d, t - 1)
                        nc.scalar.activation(hT[:], b4[:, 0, :].rearrange("p (a b) -> p a b", a=4),
                                             ACT.Copy).then_inc(s_hT, 1)
                seq(act, body, NALL - 2, NALL - 2)

            @block.vector
            def _(dve):
                ch = Chain(dve, c_tab, 17, (0, 0))
                dve.wait_ge(s_posc, 1)
                ch(nc.vector.tensor_tensor(cnt[:], run[:], C["base"], ALU.subtract))
                ch(nc.vector.tensor_tensor(above[:], cnt[:].unsqueeze(2).to_broadcast([P, E, NT]),
                                           C["thr"][:, 0:NT].unsqueeze(1).to_broadcast([P, E, NT]), ALU.is_gt))
                ch(nc.vector.tensor_reduce(ntile[:], above[:], AX.X, ALU.add))
                ch(nc.vector.tensor_tensor_scan(cum[:], ones8[:], ntile[:], 0.0, ALU.mult, ALU.add))
                ch(nc.vector.tensor_scalar(ge[:], cum[:], C["pidx"], None, ALU.is_le))
                ch(nc.vector.tensor_reduce(ei[:], ge[:], AX.X, ALU.add))
                ch(nc.vector.tensor_tensor_reduce(out=ptmp2[:], in0=ge[:], in1=ntile[:], scale=1.0, scalar=0.0,
                                                  op0=ALU.mult, op1=ALU.add, accum_out=si[:]))
                ch(nc.vector.tensor_tensor(dist[:], C["pidx"], si[:], ALU.subtract))
                ch(nc.vector.tensor_scalar(dist[:], dist[:], float(P), None, ALU.mult))
                ch(nc.vector.scalar_tensor_tensor(tabf[:, 0:1], ei[:], float(CAP), dist[:], ALU.mult, ALU.add))
                ch(nc.vector.tensor_scalar(tabf[:, 0:1], tabf[:, 0:1], float(XROWS - P), None, ALU.min))
                ch(nc.vector.tensor_scalar(tabf[:, 1:2], ei[:], float(E - 1), float(WE), ALU.min, ALU.mult))
                ch(nc.vector.tensor_tensor(tabf[:, 1:2], tabf[:, 1:2], C["shw"], ALU.add))
                nc.vector.tensor_copy(tabi[:], tabf[:]).then_inc(s_tabi, 1)
                ch(nc.vector.tensor_scalar(v0[:], run[:], C["pidx"], None, ALU.add))
                ch(nc.vector.scalar_tensor_tensor(lim[:], ntile[:], float(P), C["base"], ALU.mult, ALU.add))
                ch(nc.vector.tensor_tensor(bad[:], v0[:], lim[:], ALU.is_ge))
                ch(nc.vector.scalar_tensor_tensor(bad[:], bad[:], float(BIG), v0[:], ALU.mult, ALU.add))
                for e in range(E):
                    ins = nc.vector.tensor_scalar(padx[e][:], bad[:, e:e + 1], 1.0, None, ALU.add)
                ins.then_inc(s_pad, 1)
                ch(nc.vector.tensor_scalar(moved[:, 1:E], ntile[:, 0:E - 1], float(P), -float(CAP), ALU.mult, ALU.add))
                ch(nc.vector.memset(moved[:, 0:1], 0.0))
                ch(nc.vector.tensor_scalar(lim[:], C["base"], 1.0, None, ALU.add))
                ch(nc.vector.tensor_tensor(past[:], posall[:].unsqueeze(2).to_broadcast([P, NT, E]),
                                           lim[:].unsqueeze(1).to_broadcast([P, NT, E]), ALU.is_ge))
                ch(nc.vector.tensor_tensor(past[:], past[:], moved[:].unsqueeze(1).to_broadcast([P, NT, E]), ALU.mult))
                ch(nc.vector.tensor_reduce(shift_y[:], past[:], AX.X, ALU.add))
                nc.vector.tensor_tensor(yrow[:], shift_y[:], posall[:], ALU.add).then_inc(s_yrow, 1)

                def evac_x(tile):
                    t, p = num(tile), tile[1]
                    dve.wait_ge(s_tx, t + 1)
                    need(dve, s_u, t - 1)
                    nc.vector.tensor_copy(xT[p][:], b7[:, 0, 0:D].rearrange("p (k n) -> p k n", k=2)).then_inc(s_xT, 1)

                def hidden(tile):
                    t, p = num(tile), tile[1]
                    dve.wait_ge(s_silu, t + 1)
                    dve.wait_ge(s_u, t + 1)
                    need(dve, s_th, t - 1)
                    nc.vector.tensor_tensor(hid[p][:], bS[:, p, :], gate[:], ALU.mult).then_inc(s_h, 1)

                def result(tile, like):
                    h, p = tile
                    t = num(tile)
                    dve.wait_ge(s_d, t + 1)
                    need(dve, s_yst[p], h * 16)
                    if like < NRT:
                        nc.vector.tensor_copy(y[p][:], bX[:, p, 0:D]).then_inc(s_y, 1)
                    else:
                        hs = h - NRT // 2
                        dve.wait_ge(s_x2in[p], hs * 16 + 16)
                        nc.vector.tensor_tensor(ysum[:], x2in[p][:], bX[:, p, 0:D], ALU.add).then_inc(c_y, 1)
                        dve.wait_ge(c_y, t - NRT + 1)
                        dve.wait_ge(s_gat[p], hs * 16 + 16)
                        nc.vector.tensor_tensor(y[p][:], ysum[:], gat[p][:], ALU.add).then_inc(s_y, 1)

                def body(tile, n):
                    if n < NALL:
                        hidden(tile)
                    if n + 1 < NALL:
                        evac_x(ahead(tile))
                    if n >= 1:
                        result(back(tile, 1), n - 1)

                evac_x((0, 0))
                seq(dve, body, NRT, NRT + 2)

            @block.tensor
            def _(pe):
                pe.wait_ge(s_tab, 16)
                pe.wait_ge(s_w, 16 * (E + 1))

                def turn_in(tile):
                    h, p = tile
                    t = num(tile)
                    pe.wait_ge(s_xin[p], h * 16 + 16)
                    need(pe, s_xT, t)
                    for k in range(2):
                        ins = nc.tensor.transpose(b7[:, 0, k * P:(k + 1) * P], xin[p][:, k * P:(k + 1) * P], ident)
                    ins.then_inc(s_tx, 1)

                def up(tile, w, half, out, done):
                    p = tile[1]
                    for k in range(2):
                        ins = nc.tensor.matmul(out, xT[p][:, k, :], wexp[:, bass.ds(w + (k * 2 + half) * FF, FF)],
                                               start=(k == 0), stop=(k == 1))
                    ins.then_inc(done, 1)

                def offset(tile):
                    return pe.value_load(tabr[0:1, bass.ds(num(tile) * 2 + 1, 1)], min_val=0, max_val=E * WE)

                def body(tile, n):
                    t, p = num(tile), tile[1]
                    prev = back(tile, 1)
                    if n < NALL:
                        w = offset(tile)
                        pe.wait_ge(s_xT, t + 1)
                        need(pe, s_silu, t - 1)
                        up(tile, w, 0, bk[p][:, 0, :], s_g)
                    if n >= 1:
                        pe.wait_ge(s_h, t)
                        need(pe, s_hT, t - 1)
                        for j in range(4):
                            ins = nc.tensor.transpose(b4[:, 0, j * P:(j + 1) * P],
                                                      hid[prev[1]][:, j * P:(j + 1) * P], ident)
                        ins.then_inc(s_th, 1)
                    if n < NALL:
                        need(pe, s_h, t - 1)
                        up(tile, w, 1, bS[:, p, :], s_u)
                    if n + 1 < NALL:
                        turn_in(ahead(tile))
                    if n >= 1:
                        wp = offset(prev)
                        pe.wait_ge(s_hT, t)
                        need(pe, s_y, t - 2)
                        for j in range(4):
                            ins = nc.tensor.matmul(bX[:, prev[1], 0:D], hT[:, j, :],
                                                   wexp[:, bass.ds(wp + 4 * FF + j * D, D)],
                                                   start=(j == 0), stop=(j == 3))
                        ins.then_inc(s_d, 1)

                turn_in((0, 0))
                seq(pe, body, NALL - 2, NALL - 2)


def build(nc, arrays, ntok, nrt):
    A = {k: nc.dram_tensor(f"in_{k}", v.shape, mybir.dt.from_np(v.dtype), kind="ExternalInput").ap()
         for k, v in arrays.items()}
    A["out"] = nc.dram_tensor("out_x", (ntok, D), F32, kind="ExternalOutput").ap()
    decoder(nc, A, ntok // P, nrt)


def layout(inp):
    def parts(w):
        k = w.shape[0] // P
        return np.ascontiguousarray(w.reshape(k, P, w.shape[1]).transpose(1, 0, 2).reshape(P, -1))

    f = {k: np.asarray(v) for k, v in inp.items()}
    order = np.array([8 * (j // 4) + 4 * o + j % 4 for j in range(NPAIR) for o in range(2)])
    feat = (order[:, None] * HD + np.arange(HD)).reshape(-1)
    qkv = np.concatenate([feat, np.arange(NH * HD, (NH + 2 * NKV) * HD)])
    ntok = f["x"].shape[0] * f["x"].shape[1]
    nrt = ntok // P + E
    arrays = {
        "x": f["x"].reshape(ntok, D),
        "ctx": f["ctx_2048"].reshape(ntok, D),
        "wqkv": parts(f["L0_attn_qkv_w"][qkv].T),
        "bqkv": f["L0_attn_qkv_b"][qkv],
        "wo": parts(f["L0_attn_out_w"].T[feat]),
        "bo": f["L0_attn_out_b"],
        "sinks": np.ascontiguousarray(f["L0_attn_sinks"][order].reshape(2, 8, 2).transpose(0, 2, 1).reshape(NH)),
        "rw": parts(f["L0_ffn_router_w"].T),
        "wexp": np.stack([np.concatenate([parts(f["L0_ffn_gate_up_proj"][e]), parts(f["L0_ffn_down_proj"][e])], 1)
                          for e in range(E)] +
                         [np.concatenate([parts(np.concatenate([f["L0_ffn_shared_gate_w"], f["L0_ffn_shared_up_w"]], 1)),
                                          parts(f["L0_ffn_shared_down_w"])], 1)]),
        "const": constants(ntok, nrt),
    }
    return arrays, ntok, nrt


def kernel(**inputs):
    import concourse.bacc as bacc
    from concourse.bass_utils import run_bass_kernel_spmd

    arrays, ntok, nrt = layout(inputs)
    nc = bacc.Bacc("TRN2", target_bir_lowering=False, num_devices=1)
    build(nc, arrays, ntok, nrt)
    r = run_bass_kernel_spmd(nc, [{f"in_{k}": v for k, v in arrays.items()}], core_ids=[0])
    return r.results[0]["out_x"].reshape(np.asarray(inputs["x"]).shape)
```
